# Optimizing a Trainium2 kernel written in Bass

```python
import numpy as np
import jax
import jax.numpy as jnp

def _softmax(x, axis=-1):
    return jax.nn.softmax(x, axis=axis)

def _gelu(x):
    return jax.nn.gelu(x, approximate=True)

def _silu(x):
    return jax.nn.silu(x)

def _sigmoid(x):
    return jax.nn.sigmoid(x)

def _layernorm(x, axis=-1, eps=1e-05):
    m = jnp.mean(x, axis=axis, keepdims=True)
    v = jnp.var(x, axis=axis, keepdims=True)
    return (x - m) / jnp.sqrt(v + eps)

def _scatter_add(tgt, idx, src, axis=0):
    return tgt.at[idx].add(src)

def _segment_sum(src, seg, n):
    return jax.ops.segment_sum(src, seg, n)
kernel_name = 'mk_gnn_ffn_d1_gnn_r32_2f1114'

def setup_inputs(seed: int=0):
    np.random.seed(seed)
    _w = jnp.asarray

    def _rec_inputs():
        import jax
        import jax.numpy as jnp
        _gk = jax.random.key(seed)
        x = -0.0003713 + 1 * jax.random.normal(jax.random.fold_in(_gk, 1), (3125, 256), jnp.float32)
        src = jax.random.randint(jax.random.fold_in(_gk, 2), (50000,), 0, 3125, jnp.int32)
        dst = jnp.minimum((3125 * jax.random.uniform(jax.random.fold_in(_gk, 3), (50000,)) ** 2.0).astype(jnp.int32), 99999)
        _o = jnp.argsort(dst, stable=True)
        src = src[_o]
        dst = dst[_o]
        edge_type_8 = jax.random.randint(jax.random.fold_in(_gk, 12), (50000,), 0, 8, jnp.int32)
        return (x, src, dst, edge_type_8)
    x, src, dst, edge_type_8 = _rec_inputs()

    def _L0_gnn_setup():
        import jax, jax.numpy as jnp
        import numpy as np
        N, E, D, R, L = (50000, 250000, 256, 8, 3)
        key = jax.random.key(seed)
        k = jax.random.split(key, 7)
        scale = 1.0 / np.sqrt(D)
        x = jax.random.normal(k[0], (N, D), dtype=jnp.float32)
        edge_index = jax.random.randint(k[1], (2, E), 0, N, dtype=jnp.int64)
        edge_type = jax.random.randint(k[2], (E,), 0, R, dtype=jnp.int64)
        W_rel = jax.random.normal(k[3], (L, R, D, D), dtype=jnp.float32) * scale
        W_root = jax.random.normal(k[4], (L, D, D), dtype=jnp.float32) * scale
        bias = jax.random.normal(k[5], (L, D), dtype=jnp.float32) * 0.02
        return {'x': x, 'edge_index': edge_index, 'edge_type': edge_type, 'W_rel': W_rel, 'W_root': W_root, 'bias': bias}
    _L0_gnn_all = _L0_gnn_setup()
    _L0_gnn_in = {k: v for k, v in _L0_gnn_all.items() if k in ('W_rel', 'W_root', 'bias')}
    del _L0_gnn_all

    def _L0_ffn_setup():
        import jax, jax.numpy as jnp
        import numpy as np
        D_MODEL = 256
        EXPERT_DIM = 512
        NUM_EXPERTS = 8
        TOP_K = 2
        SEQ_LEN = 64
        BATCH = 2
        key = jax.random.key(seed)
        ks = jax.random.split(key, 8)
        s = 0.02
        x = jax.random.normal(ks[0], (SEQ_LEN, BATCH, D_MODEL), dtype=jnp.float32)
        Wg = jax.random.normal(ks[1], (D_MODEL, NUM_EXPERTS), dtype=jnp.float32) * s
        bg = jax.random.normal(ks[2], (NUM_EXPERTS,), dtype=jnp.float32) * s
        bias = jnp.zeros((NUM_EXPERTS,), dtype=jnp.float32)
        W1 = jax.random.normal(ks[3], (NUM_EXPERTS, D_MODEL, EXPERT_DIM), dtype=jnp.float32) * s
        b1 = jax.random.normal(ks[4], (NUM_EXPERTS, EXPERT_DIM), dtype=jnp.float32) * s
        W2 = jax.random.normal(ks[5], (NUM_EXPERTS, EXPERT_DIM, D_MODEL), dtype=jnp.float32) * s
        b2 = jax.random.normal(ks[6], (NUM_EXPERTS, D_MODEL), dtype=jnp.float32) * s
        return {'x': x, 'Wg': Wg, 'bg': bg, 'bias': bias, 'W1': W1, 'b1': b1, 'W2': W2, 'b2': b2}
    _L0_ffn_all = _L0_ffn_setup()
    _L0_ffn_in = {k: v for k, v in _L0_ffn_all.items() if k in ('Wg', 'bg', 'bias', 'W1', 'b1', 'W2', 'b2')}
    del _L0_ffn_all
    return {'x': x, 'src': src, 'dst': dst, 'edge_type_8': edge_type_8, 'L0_gnn_W_rel': _L0_gnn_in['W_rel'], 'L0_gnn_W_root': _L0_gnn_in['W_root'], 'L0_gnn_bias': _L0_gnn_in['bias'], 'L0_ffn_Wg': _L0_ffn_in['Wg'], 'L0_ffn_bg': _L0_ffn_in['bg'], 'L0_ffn_bias': _L0_ffn_in['bias'], 'L0_ffn_W1': _L0_ffn_in['W1'], 'L0_ffn_b1': _L0_ffn_in['b1'], 'L0_ffn_W2': _L0_ffn_in['W2'], 'L0_ffn_b2': _L0_ffn_in['b2']}

def reference(x, src, dst, edge_type_8, L0_gnn_W_rel, L0_gnn_W_root, L0_gnn_bias, L0_ffn_Wg, L0_ffn_bg, L0_ffn_bias, L0_ffn_W1, L0_ffn_b1, L0_ffn_W2, L0_ffn_b2):
    import jax
    import jax.numpy as jnp

    def _L0_gnn_ref(x, edge_index, edge_type, W_rel, W_root, bias):
        import jax, jax.numpy as jnp
        import numpy as np
        N, E, D, R, L = (50000, 250000, 256, 8, 3)
        src, dst = (edge_index[0], edge_index[1])
        n_layers = W_rel.shape[0]
        for l in range(n_layers):
            xr = jnp.einsum('nd,rde->rne', x, W_rel[l])
            msg = xr[edge_type, src]
            agg = jax.ops.segment_sum(msg, dst, num_segments=x.shape[0])
            x = jax.nn.relu(agg + x @ W_root[l] + bias[l])
        return x

    def _L0_ffn_ref(x, Wg, bg, bias, W1, b1, W2, b2):
        import jax, jax.numpy as jnp
        import numpy as np
        D_MODEL = 256
        EXPERT_DIM = 512
        NUM_EXPERTS = 8
        TOP_K = 2
        SEQ_LEN = 64
        BATCH = 2
        x_flat = x.reshape(-1, D_MODEL)
        gate_logits = x_flat @ Wg + bg + bias
        topk_vals, topk_idx = jax.lax.top_k(gate_logits, TOP_K)
        topk_w = jax.nn.softmax(topk_vals, axis=-1)
        combine = (jax.nn.one_hot(topk_idx, NUM_EXPERTS, dtype=x.dtype) * topk_w[..., None]).sum(axis=1)
        h = jax.nn.relu(jnp.einsum('td,edh->teh', x_flat, W1) + b1)
        y = jnp.einsum('teh,ehd->ted', h, W2) + b2
        out = jnp.einsum('ted,te->td', y, combine)
        return out.reshape(x.shape)
    edge_index = jnp.stack([src, dst])
    x = x + _L0_gnn_ref(_layernorm(x, axis=-1), edge_index, edge_type_8, L0_gnn_W_rel, L0_gnn_W_root, L0_gnn_bias)
    x = x + _L0_ffn_ref(_layernorm(x, axis=-1)[None], L0_ffn_Wg, L0_ffn_bg, L0_ffn_bias, L0_ffn_W1, L0_ffn_b1, L0_ffn_W2, L0_ffn_b2)[0]
    return x

_drawn_inputs = setup_inputs


def setup_inputs(seed=0):
    import zlib

    import numpy as np

    out = dict(_drawn_inputs(seed))
    spreads = {'L0_ffn_bias': (0.0, 0.8)}
    factors = {'L0_gnn_bias': 8.0,
     'L0_ffn_Wg': 8.0,
     'L0_ffn_bg': 55.361,
     'L0_ffn_W1': 8.0,
     'L0_ffn_b1': 64.0,
     'L0_ffn_W2': 8.0,
     'L0_ffn_b2': 200.0}
    for name, (base, spread) in spreads.items():
        noise = np.random.default_rng([zlib.crc32(name.encode()), seed]).standard_normal(out[name].shape)
        drawn = base * np.exp(spread * noise) if base else spread * noise
        out[name] = jnp.asarray(drawn.astype(out[name].dtype))
    for name, factor in factors.items():
        out[name] = (out[name] * factor).astype(out[name].dtype)
    return out
```

```python
import concourse.bass as bass
from concourse import mybir
from contextlib import ExitStack


def build_rgcn_moe(nc, x, src, dst, etype, w_rel, w_root, g_bias, wg, bg, gate_bias, w1, b1, w2, b2, out):
    F32 = mybir.dt.float32
    F16 = mybir.dt.float16
    I32 = mybir.dt.int32
    U32 = mybir.dt.uint32
    ALU = mybir.AluOpType
    ACT = mybir.ActivationFunctionType
    AX = mybir.AxisListType
    ds = bass.ds

    P = 128
    N, D = x.shape
    E = src.shape[0]
    L, R = w_rel.shape[0], w_rel.shape[1]
    NE, H = w1.shape[0], w1.shape[2]
    KD = D // P
    KH = H // P
    NT = -(-N // P)
    LAST = N - (NT - 1) * P
    EP = 125
    ET = E // EP
    assert EP * ET == E
    UA = 8
    NC = -(-(-(-E // P) + NT) // (2 * UA)) * (2 * UA)
    CAP = 4096
    UD = 5
    assert NT % UD == 0 and NC <= 512
    JD = NT // UD
    TU = R * D // 512
    SS = 10
    assert UD * TU % SS == 0
    SPI = UD * TU // SS
    UP = 4
    G = 5
    NG = NT // G
    HB = G * P // 2
    EPS = 1e-5

    table = nc.dram_tensor("table", (NT * P * R, D), F32, kind="Internal").ap()
    table_units = table.rearrange("(n u r) d -> u n (r d)", u=TU, r=R // TU)

    ctx = ExitStack()
    with ctx:
        def sb(name, shape, dt=F32):
            return ctx.enter_context(nc.sbuf_tensor(name, shape, dt))

        def sem(name):
            return ctx.enter_context(nc.semaphore(name))

        acc = sb("acc", [P, NT * D])
        scratch = sb("scratch", [P, 2 * NT * ET])
        xr = sb("xr", [P, UD, D])
        xt = sb("xt", [P, UD, KD, P])
        stage = sb("stage", [P, SS, 512])
        wr = sb("wr", [P, KD, R, D])
        wroot = sb("wroot", [P, KD, D])
        gbT = sb("gbT", [P, L, KD])
        gb_last = sb("gb_last", [P, D])
        msg = sb("msg", [P, UA, D])
        onehot = sb("onehot", [P, UA, P])
        ident = sb("ident", [P, P])
        iota_p1 = sb("iota_p1", [P, P])
        idx = sb("idx", [P, NC], I32)
        dlp = sb("dlp", [P, NC])
        idx_now = sb("idx_now", [P, 2, UA], I32)
        owner = sb("owner", [1, NC], I32)
        stats = sb("stats", [P, 6 * NT])
        mv = sb("mv", [P, NT, 2])
        rstd = sb("rstd", [P, NT])
        eps_t = sb("eps_t", [P, 1])
        small = sb("small", [P, 12 * NT])
        e_src = sb("e_src", [EP, ET], I32)
        e_dst = sb("e_dst", [EP, ET], I32)
        e_typ = sb("e_typ", [EP, ET], I32)
        e_tmp = sb("e_tmp", [EP, ET], I32)
        e_tile = sb("e_tile", [EP, ET])
        e_lo = sb("e_lo", [EP, ET])
        e_hi = sb("e_hi", [EP, ET])
        v_lo = sb("v_lo", [EP, ET])
        v_hi = sb("v_hi", [EP, ET])
        iota_c = sb("iota_c", [P, NC], F16)
        iota_s = sb("iota_s", [P, P], F16)
        iota_g = sb("iota_g", [P, NT])
        iota_row = sb("iota_row", [1, NC])
        tri = sb("tri", [P, P])
        ones = sb("ones", [P, P])
        zero16 = sb("zero16", [P, P], F16)
        pick_c = sb("pick_c", [EP, UP, NC], F16)
        pick_s = sb("pick_s", [EP, UP, 2, P], F16)

        acc_t = acc[:, :].rearrange("p (t d) -> p t d", d=D)
        member = scratch[0:EP, 0:NT * ET]
        member_gt = member.rearrange("p (g t) -> p g t", t=ET)
        rank = scratch[0:EP, NT * ET:2 * NT * ET]
        rank_gt = rank.rearrange("p (g t) -> p g t", t=ET)
        own_cmp = scratch[0:1, 0:NC * NT].rearrange("p (c g) -> p c g", g=NT)

        def psum(name):
            return ctx.enter_context(nc.psum_tensor(name, [P, 512], F32))
        ps_t = [psum(f"ps_t{i}") for i in range(4)]
        ps_a = [psum(f"ps_a{i}") for i in range(2)]
        ps_root = psum("ps_root")
        ps_x = psum("ps_x")

        s_x = sem("x_landed")
        s_edges = sem("edges_landed")
        s_w = sem("layer_weights_landed")
        s_b = sem("biases_landed")
        s_const = sem("constants_made")
        s_cst0 = sem("constants_cleared")
        s_dve = sem("vector_step_done")
        s_var = sem("variances_ready")
        s_std = sem("stds_ready")
        s_normed = sem("normed_rows_ready")
        s_cnt = sem("edge_counts_ready")
        s_base = sem("count_sums_ready")
        s_pick = sem("picks_ready")
        s_moved = sem("picks_used")
        s_sorted = sem("records_sorted")
        s_tables = sem("sorted_tables_ready")
        s_row = sem("rows_copied")
        s_tr = sem("rows_transposed")
        s_xt = sem("xt_ready")
        s_unit = sem("units_multiplied")
        s_copied = sem("units_copied")
        s_sent = [sem(f"stage_sent{i}") for i in range(SS)]
        s_table = sem("tables_written")
        s_root = sem("roots_multiplied")
        s_rootc = sem("roots_copied")
        s_gb = sem("layer_bias_ready")
        s_idx = sem("chunk_indices_ready")
        s_got = [sem(f"messages_landed{i}") for i in range(UA)]
        s_oh = sem("onehots_ready")
        s_sum = sem("chunks_summed")
        s_add = sem("chunks_added")

        s_x2 = sem("x_again_landed")
        s_xpad = sem("x_again_padding_cleared")
        s_var2 = sem("variances2_ready")
        s_std2 = sem("stds2_ready")
        s_n2 = sem("tokens_normed")
        s_tr2 = sem("tokens_transposed")
        s_tt = sem("tokens_t_ready")
        s_gw = sem("gate_weights_landed")
        s_tok = sem("tokens_stored")
        s_logit = sem("logits_ready")
        s_gap = sem("gate_gap_ready")
        s_exp = sem("gate_exp_ready")
        s_ew = [sem(f"expert_weights_landed{i}") for i in range(2)]
        s_h = sem("hidden_multiplied")
        s_b1 = sem("expert_bias_ready")
        s_hc = sem("hidden_ready")
        s_y = sem("outputs_multiplied")
        s_yc = sem("outputs_read")
        s_res = sem("outputs_added")
        s_out = sem("result_written")

        class Carve:
            at = 0

            def __call__(self, n):
                v = scratch[:, self.at:self.at + n]
                self.at += n
                return v
        carve = Carve()
        x_again = carve(NT * D).rearrange("p (t d) -> p t d", d=D)
        tokT = carve(KD * NT * P).rearrange("p (k n) -> p k n", k=KD)
        hT = carve(KH * G * P).rearrange("p (k n) -> p k n", k=KH)
        b2_b = carve(NE * D).rearrange("p (e d) -> p e d", d=D)
        ycopy = carve(G * D).rearrange("p (b d) -> p b d", d=D)
        gate = [carve(NT * NE).rearrange("p (t e) -> p t e", e=NE) for _ in range(5)]
        assert carve.at <= 2 * NT * ET
        w1_s = wr[:, :, :, :].rearrange("p k r d -> p (k r d)")[:, 0:2 * KD * H].rearrange(
            "p (b k h) -> p b k h", b=2, k=KD)
        w2_s = wr[:, :, :, :].rearrange("p k r d -> p (k r d)")[:, 2 * KD * H:2 * KD * H + 2 * KH * D].rearrange(
            "p (b k d) -> p b k d", b=2, k=KH)
        wg_s = sb("wg_s", [P, KD, NE])
        b1_s = sb("b1_s", [P, NE, KH])
        gvec = sb("gvec", [P, 2, NE])
        gcol = sb("gcol", [P, 8, NT])
        iota_e = sb("iota_e", [P, NE])
        gb_now = sb("gb_now", [P, KD])
        b1_now = sb("b1_now", [P, KH])

        block = ctx.enter_context(nc.Block())

        x_main = x[0:(NT - 1) * P, :].rearrange("(t p) d -> p t d", p=P)
        out_main = out[0:(NT - 1) * P, :].rearrange("(t p) d -> p t d", p=P)
        w_rel_k = w_rel.rearrange("l r (k p) e -> l k p r e", p=P)
        w_root_k = w_root.rearrange("l (k p) e -> l k p e", p=P)

        def layers_after_first(eng, body):
            with eng.Fori(1, L) as l:
                body(l)

        @block.sync
        def _(sp):
            sp.dma_start(acc_t[:, 0:NT - 1, :], x_main).then_inc(s_x, 16)
            sp.wait_ge(s_cst0, 1)
            sp.dma_start(acc_t[0:LAST, NT - 1, :], x[(NT - 1) * P:N, :]).then_inc(s_x, 16)
            for buf, arr in ((e_src, src), (e_dst, dst), (e_typ, etype)):
                sp.dma_start(buf[:, :], arr.rearrange("(p t) -> p t", p=EP)).then_inc(s_edges, 16)

            def load_layer(l):
                for k in range(KD):
                    sp.dma_start(wr[:, k, :, :], w_rel_k[ds(l, 1), k, :, :, :].rearrange("o p r e -> p (o r) e"))\
                      .then_inc(s_w, 16)
                    sp.dma_start(wroot[:, k, :], w_root_k[ds(l, 1), k, :, :].rearrange("o p e -> p (o e)"))\
                      .then_inc(s_w, 16)
            load_layer(0)

            def send_units(l):
                with sp.Fori(0, JD) as j:
                    for u in range(UD):
                        for q in range(TU):
                            n = l * NT + j * UD + u
                            k = u * TU + q
                            sp.wait_ge(s_copied, n * TU + (q + 1 + TU))
                            sp.dma_start(table_units[q, ds((j * UD + u) * P, P), :],
                                         stage[:, k % SS, :]).then_inc(s_sent[k % SS], 16)
                for s in range(SS):
                    sp.wait_ge(s_sent[s], 16 * SPI * JD * (l + 1))
                sp.sem_inc(s_table, 1)
            send_units(0)
            sp.wait_ge(s_tables, 1)
            sp.dma_start(x_again[:, 0:NT - 1, :], x_main).then_inc(s_x2, 16)
            sp.wait_ge(s_xpad, 1)
            sp.dma_start(x_again[0:LAST, NT - 1, :], x[(NT - 1) * P:N, :]).then_inc(s_x2, 16)
            for l in range(1, L):
                sp.wait_ge(s_root, NT * l)
                load_layer(l)
                send_units(l)
            def load_expert(e, b):
                sp.dma_start(w1_s[:, b, :, :], w1[ds(e, 1), :, :].rearrange("o (k p) h -> p (o k) h", p=P))\
                  .then_inc(s_ew[b], 16)
                sp.dma_start(w2_s[:, b, :, :], w2[ds(e, 1), :, :].rearrange("o (k p) d -> p (o k) d", p=P))\
                  .then_inc(s_ew[b], 16)

            sp.wait_ge(s_root, NT * L)
            for e in range(2):
                load_expert(e, e)
            with sp.Fori(1, NE // 2) as pair:
                for b in range(2):
                    e = pair * 2
                    sp.wait_ge(s_y, (e + (b - 1)) * NT)
                    load_expert(pair * 2 + b, b)
            for g in range(NG):
                sp.wait_ge(s_res, NT * (NE - 1) + G * (g + 1))
                t0, t1 = g * G, min((g + 1) * G, NT - 1)
                sp.dma_start(out_main[:, t0:t1, :], acc_t[:, t0:t1, :]).then_inc(s_out, 16)
            sp.dma_start(out[(NT - 1) * P:N, :], acc_t[0:LAST, NT - 1, :]).then_inc(s_out, 16)
            sp.wait_ge(s_out, 16 * (NG + 1))

        @block.gpsimd
        def _(pool):
            pool.sem_inc(s_tok, 1)
            nc.gpsimd.memset(acc_t[:, NT - 1, :], 0.0).then_inc(s_cst0, 1)
            nc.gpsimd.memset(ident[:, :], 0.0).then_inc(s_cst0, 1)
            nc.gpsimd.memset(ones[:, :], 1.0).then_inc(s_cst0, 1)
            nc.gpsimd.memset(zero16[:, :], 0.0).then_inc(s_const, 1)
            nc.gpsimd.iota(iota_p1[:, :], [[1, P]], base=1, channel_multiplier=0,
                           allow_small_or_imprecise_dtypes=True).then_inc(s_const, 1)
            nc.gpsimd.iota(iota_c[:, :], [[1, NC]], base=0, channel_multiplier=0,
                           allow_small_or_imprecise_dtypes=True).then_inc(s_const, 1)
            nc.gpsimd.iota(iota_g[:, :], [[1, NT]], base=0, channel_multiplier=0,
                           allow_small_or_imprecise_dtypes=True).then_inc(s_const, 1)
            nc.gpsimd.iota(iota_row[:, :], [[1, NC]], base=0, channel_multiplier=0,
                           allow_small_or_imprecise_dtypes=True).then_inc(s_const, 1)
            nc.gpsimd.iota(iota_s[:, :], [[1, P]], base=1, channel_multiplier=0,
                           allow_small_or_imprecise_dtypes=True).then_inc(s_const, 1)
            nc.gpsimd.iota(iota_e[:, :], [[-1, NE]], base=NE, channel_multiplier=0,
                           allow_small_or_imprecise_dtypes=True).then_inc(s_const, 1)
            pool.wait_ge(s_cst0, 3)
            nc.gpsimd.affine_select(out=ident[:, :], in_=ident[:, :], compare_op=ALU.not_equal, fill=1.0,
                                    base=0, pattern=[[-1, P]], channel_multiplier=1).then_inc(s_const, 1)
            nc.gpsimd.affine_select(out=tri[:, :], in_=ones[:, :], compare_op=ALU.is_gt, fill=0.0,
                                    base=0, pattern=[[1, P]], channel_multiplier=-1).then_inc(s_const, 1)

            with nc.allow_non_contiguous_dma(reason="a few hundred bias values"):
                nc.gpsimd.dma_start(gbT[:, :, :], g_bias.rearrange("l (k p) -> p l k", p=P)).then_inc(s_b, 16)
                nc.gpsimd.dma_start(b1_s[:, :, :], b1.rearrange("e (k p) -> p e k", p=P)).then_inc(s_gw, 16)
            nc.gpsimd.dma_start(gb_last[:, :], g_bias[L - 1:L, :].to_broadcast([P, D])).then_inc(s_b, 16)
            nc.gpsimd.dma_start(wg_s[:, :, :], wg.rearrange("(k p) e -> p k e", p=P)).then_inc(s_gw, 16)
            nc.gpsimd.dma_start(gvec[:, 0, :], bg.rearrange("(o e) -> o e", o=1).to_broadcast([P, NE]))\
                .then_inc(s_gw, 16)
            nc.gpsimd.dma_start(gvec[:, 1, :], gate_bias.rearrange("(o e) -> o e", o=1).to_broadcast([P, NE]))\
                .then_inc(s_gw, 16)

            def copy_rows(l):
                with pool.Fori(0, JD) as j:
                    for u in range(UD):
                        n = l * NT + j * UD + u
                        if u == 0:
                            pool.wait_ge(s_normed, 1)
                            pool.wait_ge(s_add, l * NC + 2)
                        pool.wait_ge(s_tr, n + 1)
                        nc.gpsimd.tensor_copy(xr[:, u, :], acc[:, ds((j * UD + u) * D, D)]).then_inc(s_row, 1)

            def gather(l):
                with pool.Fori(0, NC // (2 * UA)) as j:
                    for b in range(2):
                        if b == 0:
                            pool.wait_ge(s_table, l + 1)
                        pool.wait_ge(s_idx, l * (NC // UA) + j * 2 + (b + 1))
                        for u in range(UA):
                            pool.wait_ge(s_sum, (l * NC) + j * (2 * UA) + (b * UA + u + 1))
                            nc.gpsimd.indirect_dma_start(
                                out=msg[:, u, :], out_offset=None, in_=table[:, :],
                                in_offset=bass.IndirectOffsetOnAxis(ap=idx_now[:, b, u:u + 1].bitcast(U32), axis=0),
                                bounds_check=j * (2 * UA) + (b * UA + u + N * R - 1), oob_is_err=False).then_inc(s_got[u], 16)

            pool.wait_ge(s_normed, 1)
            copy_rows(0)
            pool.wait_ge(s_tables, 1)
            nc.gpsimd.memset(x_again[:, NT - 1, :], 0.0).then_inc(s_xpad, 1)
            nc.gpsimd.dma_start(b2_b.rearrange("p e d -> p (e d)"),
                                b2.rearrange("(o e) d -> o (e d)", o=1).to_broadcast([P, NE * D])).then_inc(s_gw, 16)
            gather(0)

            def later(l):
                copy_rows(l)
                gather(l)
            layers_after_first(pool, later)
            with pool.Fori(0, NG) as g:
                for u in range(G):
                    pool.wait_ge(s_tt, g * G + (u + 2))
                    nc.gpsimd.tensor_copy(tokT[:, :, ds((g * G + u) * P, P)], xt[:, u, :, :]).then_inc(s_tok, 1)

        @block.scalar
        def _(act):
            nc.scalar.sem_inc(s_copied, TU)
            nc.scalar.sem_inc(s_xt, 1)
            nc.scalar.sem_inc(s_tt, 1)
            nc.scalar.sem_inc(s_rootc, 1)
            act.wait_ge(s_var, 1)
            nc.scalar.activation(rstd[:, :], mv[:, :, 1], ACT.Sqrt, bias=eps_t[:, :], scale=1.0).then_inc(s_std, 1)

            def dense_tiles(l, j, first):
                def tile_t(u):
                    n = l * NT + j * UD + u
                    act.wait_ge(s_tr, n + (1 + UD))
                    for k in range(KD):
                        src_ps = ps_x[:, k * P:(k + 1) * P]
                        if first:
                            i = nc.scalar.copy(xt[:, u, k, :], src_ps)
                        else:
                            i = nc.scalar.activation(xt[:, u, k, :], src_ps, ACT.Relu,
                                                     bias=gb_now[:, k:k + 1])
                    i.then_inc(s_xt, 1)

                def units(u):
                    n = l * NT + j * UD + u
                    for q in range(TU):
                        k = u * TU + q
                        act.wait_ge(s_unit, n * TU + (q + 1))
                        uses = (l * JD + j) * SPI + k // SS
                        if not isinstance(uses, int) or uses > 0:
                            act.wait_ge(s_sent[k % SS], uses * 16)
                        nc.scalar.copy(stage[:, k % SS, :], ps_t[q][:, :]).then_inc(s_copied, 1)
                    act.wait_ge(s_root, n + 1)
                    nc.scalar.copy(acc[:, ds((j * UD + u) * D, D)], ps_root[:, 0:D]).then_inc(s_rootc, 1)
                tile_t(0)
                for u in range(1, UD):
                    tile_t(u)
                    units(u - 1)
                units(UD - 1)

            def dense(l, start, first):
                with act.Fori(start, JD) as j:
                    dense_tiles(l, j, first)

            def index_chunks(l):
                with act.Fori(0, NC // (2 * UA)) as j:
                    for b in range(2):
                        act.wait_ge(s_sum, l * NC + j * (2 * UA) + (b * UA + 1))
                        nc.scalar.copy(idx_now[:, b, :], idx[:, ds(j * (2 * UA) + b * UA, UA)]).then_inc(s_idx, 1)

            dense_tiles(0, 0, True)
            dense(0, 1, True)
            act.wait_ge(s_b, 32)
            act.wait_ge(s_tables, 1)
            index_chunks(0)

            def later(l):
                act.wait_ge(s_rootc, l * NT + 1)
                nc.scalar.copy(gb_now[:, :], gbT[:, ds(l - 1, 1), :].rearrange("p o k -> p (o k)"))\
                    .then_inc(s_gb, 1)
                act.wait_ge(s_gb, l)
                act.wait_ge(s_tables, 1)
                dense(l, 0, False)
                index_chunks(l)
            layers_after_first(act, later)

            with act.Fori(0, NG) as g:
                act.wait_ge(s_var2, g + 1)
                nc.scalar.activation(rstd[:, 0:G], mv[:, 0:G, 1], ACT.Sqrt,
                                     bias=eps_t[:, :], scale=1.0).then_inc(s_std2, 1)
                for u in range(G):
                    t = g * G + u
                    act.wait_ge(s_tr2, t + (1 + G))
                    act.wait_ge(s_tok, g * G + 1)
                    act.wait_ge(s_logit, g * G + 1)
                    nc.scalar.copy(xt[:, u, :, :], ps_x[:, 0:D].rearrange(
                        "p (k n) -> p k n", k=KD)).then_inc(s_tt, 1)
            act.wait_ge(s_gap, 1)
            nc.scalar.activation(gcol[:, 3, :], gcol[:, 2, :], ACT.Exp).then_inc(s_exp, 1)
            nc.scalar.sem_inc(s_hc, KH)
            act.wait_ge(s_gw, 80)
            with act.Fori(0, NE) as e:
                act.wait_ge(s_hc, e * (NG * 2 * KH) + KH)
                nc.scalar.copy(b1_now[:, :], b1_s[:, ds(e, 1), :].rearrange("p o k -> p (o k)")).then_inc(s_b1, 1)
                act.wait_ge(s_b1, e + 1)
                act.wait_ge(s_gw, 80)
                with act.Fori(0, NG) as g:
                    for half in range(2):
                        for m in range(KH):
                            q = half * KH + m
                            act.wait_ge(s_h, (e * NG + g) * (2 * KH) + (q + 1))
                            nc.scalar.activation(hT[:, m, half * HB:(half + 1) * HB], ps_t[m][:, 0:HB], ACT.Relu,
                                                 bias=b1_now[:, m:m + 1]).then_inc(s_hc, 1)

        @block.vector
        def _(dve):
            steps = [0]

            def link(i):
                steps[0] += 1
                i.then_inc(s_dve, 1)
                dve.wait_ge(s_dve, steps[0])
                return i

            V = nc.vector
            V.sem_inc(s_yc, 1)
            V.sem_inc(s_add, 2)
            link(V.memset(eps_t[:, :], EPS))
            dve.wait_ge(s_x, 32)
            for t in range(NT):
                i = V.bn_stats(stats[:, 6 * t:6 * t + 6], acc_t[:, t, :])
            link(i)
            for t in range(NT):
                i = V.bn_aggr(mv[:, t, :], stats[:, 6 * t:6 * t + 6])
            i.then_inc(s_var, 1)
            dve.wait_ge(s_std, 1)
            link(V.reciprocal(rstd[:, :], rstd[:, :]))
            for t in range(NT):
                i = V.tensor_scalar(acc_t[:, t, :], acc_t[:, t, :], mv[:, t, 0:1], rstd[:, t:t + 1],
                                    ALU.subtract, ALU.mult)
            i.then_inc(s_normed, 1)

            dve.wait_ge(s_edges, 48)
            dve.wait_ge(s_const, 9)
            link(V.tensor_scalar(e_tmp[:, :], e_dst[:, :], 7, None, ALU.arith_shift_right))
            link(V.tensor_copy(e_tile[:, :], e_tmp[:, :]))
            link(V.tensor_scalar(e_tmp[:, :], e_dst[:, :], 127, None, ALU.bitwise_and))
            link(V.tensor_copy(e_lo[:, :], e_tmp[:, :]))
            link(V.tensor_copy(v_hi[:, :], e_src[:, :]))
            link(V.tensor_copy(v_lo[:, :], e_typ[:, :]))
            link(V.scalar_tensor_tensor(v_hi[:, :], v_hi[:, :], float(R), v_lo[:, :], ALU.mult, ALU.add))
            link(V.scalar_tensor_tensor(v_hi[:, :], v_hi[:, :], 256.0, e_lo[:, :], ALU.mult, ALU.add))
            link(V.tensor_scalar(e_src[:, :], v_hi[:, :], 1.0, None, ALU.add))
            link(V.tensor_scalar(e_tmp[:, :], e_src[:, :], 12, None, ALU.arith_shift_right))
            link(V.tensor_copy(v_hi[:, :], e_tmp[:, :]))
            link(V.tensor_scalar(e_tmp[:, :], e_src[:, :], CAP - 1, None, ALU.bitwise_and))
            link(V.tensor_scalar(v_lo[:, :], e_tmp[:, :], float(-CAP // 2), None, ALU.add))
            link(V.tensor_tensor(member_gt, e_tile[:, :].unsqueeze(1).to_broadcast([EP, NT, ET]),
                                 iota_g[0:EP, :].unsqueeze(2).to_broadcast([EP, NT, ET]), ALU.is_equal))
            link(V.tensor_tensor_scan(rank, member, member, 0.0, ALU.add, ALU.max))
            cum = small[0:EP, 0:NT]
            cnt = small[0:EP, NT:2 * NT]
            before = small[0:EP, 2 * NT:3 * NT]
            link(V.tensor_copy(cum, rank_gt[:, :, ET - 1]))
            link(V.memset(before[:, 0:1], 0.0))
            link(V.tensor_copy(before[:, 1:NT], cum[:, 0:NT - 1]))
            V.tensor_tensor(cnt, cum, before, ALU.subtract).then_inc(s_cnt, 1)
            dve.wait_ge(s_base, 1)
            totals = small[:, 3 * NT:4 * NT]
            tmp_i = small[:, 4 * NT:5 * NT].bitcast(I32)
            chunks = small[:, 5 * NT:6 * NT]
            ends = small[:, 6 * NT:7 * NT]
            shift = small[0:EP, 7 * NT:8 * NT]
            link(V.tensor_scalar(tmp_i, ps_a[0][:, NT:2 * NT], float(P - 1), None, ALU.add))
            link(V.tensor_scalar(tmp_i, tmp_i, 7, None, ALU.arith_shift_right))
            link(V.tensor_scalar(chunks, tmp_i, 1.0, None, ALU.max))
            link(V.tensor_tensor_scan(ends, chunks, chunks, 0.0, ALU.add, ALU.max))
            link(V.tensor_tensor(totals, ends, chunks, ALU.subtract))
            link(V.tensor_tensor(before, ps_a[0][0:EP, 0:NT], before, ALU.subtract))
            link(V.scalar_tensor_tensor(shift, totals[0:EP, :], float(P), before, ALU.mult, ALU.add))
            link(V.tensor_tensor(rank_gt, rank_gt, shift.unsqueeze(2).to_broadcast([EP, NT, ET]), ALU.add))
            link(V.tensor_tensor(rank, rank, member, ALU.mult))
            link(V.tensor_reduce(e_lo[:, :], rank_gt.rearrange("p g t -> p t g"), AX.X, ALU.add))
            link(V.tensor_scalar(e_src[:, :], e_lo[:, :], -1.0, None, ALU.add))
            link(V.tensor_scalar(e_tmp[:, :], e_src[:, :], 7, None, ALU.arith_shift_right))
            link(V.tensor_copy(e_hi[:, :], e_tmp[:, :]))
            link(V.tensor_scalar(e_tmp[:, :], e_src[:, :], 127, None, ALU.bitwise_and))
            link(V.tensor_scalar(e_lo[:, :], e_tmp[:, :], 1.0, None, ALU.add))
            link(V.tensor_tensor(own_cmp, iota_row[:, :].unsqueeze(2).to_broadcast([1, NC, NT]),
                                 ends[0:1, :].unsqueeze(1).to_broadcast([1, NC, NT]), ALU.is_ge))
            link(V.tensor_reduce(iota_row[:, :], own_cmp, AX.X, ALU.add))
            link(V.tensor_scalar(owner[:, :], iota_row[:, :], float(NT - 1), float(D), ALU.min, ALU.mult))
            with dve.Fori(0, ET // UP) as j:
                for u in range(UP):
                    t = j * UP + u
                    dve.wait_ge(s_moved, t + 1)
                    V.tensor_scalar(pick_c[:, u, :], iota_c[0:EP, :], e_hi[:, ds(t, 1)], None, ALU.is_equal)
                    V.tensor_scalar(pick_s[:, u, 0, :], iota_s[0:EP, :], e_lo[:, ds(t, 1)], v_hi[:, ds(t, 1)],
                                    ALU.is_equal, ALU.mult)
                    V.tensor_scalar(pick_s[:, u, 1, :], iota_s[0:EP, :], e_lo[:, ds(t, 1)], v_lo[:, ds(t, 1)],
                                    ALU.is_equal, ALU.mult).then_inc(s_pick, 1)
            dve.wait_ge(s_sorted, 1)
            link(V.tensor_scalar(dlp[:, :], ps_a[1][:, 0:NC], float(CAP // 2), None, ALU.add))
            link(V.scalar_tensor_tensor(idx[:, :], ps_a[0][:, 0:NC], float(CAP), dlp[:, :], ALU.mult, ALU.add))
            tmp = scratch[:, 0:NC].bitcast(I32)
            link(V.tensor_scalar(tmp, idx[:, :], 255, None, ALU.bitwise_and))
            link(V.tensor_copy(dlp[:, :], tmp))
            link(V.tensor_scalar(idx[:, :], idx[:, :], 8, None, ALU.arith_shift_right))
            V.sem_inc(s_tables, 1)

            def aggregate(l):
                with dve.Fori(0, NC // UA) as j:
                    def build(u):
                        n = l * NC + j * UA + u
                        dve.wait_ge(s_sum, n + 1)
                        V.tensor_scalar(onehot[:, u, :], iota_p1[:, :], dlp[:, ds(j * UA + u, 1)], None,
                                        ALU.is_equal).then_inc(s_oh, 1)

                    def add(u):
                        n = l * NC + j * UA + u
                        at = dve.value_load(owner[0:1, ds(j * UA + u, 1)], min_val=0, max_val=(NT - 1) * D)
                        if u == 0:
                            dve.wait_ge(s_rootc, l * NT + (NT + 1))
                        dve.wait_ge(s_sum, n + (1 + UA))
                        dve.wait_ge(s_add, n + 2)
                        V.tensor_tensor(acc[:, ds(at, D)], acc[:, ds(at, D)], ps_a[u % 2][:, 0:D], ALU.add)\
                            .then_inc(s_add, 1)
                    build(0)
                    for u in range(1, UA):
                        build(u)
                        add(u - 1)
                    add(UA - 1)
            aggregate(0)
            layers_after_first(dve, aggregate)

            dve.wait_ge(s_b, 32)
            dve.wait_ge(s_x2, 32)
            dve.wait_ge(s_add, L * NC + 2)
            for g in range(NG):
                rows = acc_t[:, g * G:(g + 1) * G, :]
                link(V.tensor_tensor(rows, rows, gb_last[:, :].unsqueeze(1).to_broadcast([P, G, D]), ALU.add))
                link(V.scalar_tensor_tensor(rows, rows, 0.0, x_again[:, g * G:(g + 1) * G, :], ALU.max, ALU.add))
                for u in range(G):
                    i = V.bn_stats(stats[:, 6 * u:6 * u + 6], acc_t[:, g * G + u, :])
                link(i)
                for u in range(G):
                    i = V.bn_aggr(mv[:, u, :], stats[:, 6 * u:6 * u + 6])
                i.then_inc(s_var2, 1)
                dve.wait_ge(s_std2, g + 1)
                link(V.reciprocal(rstd[:, 0:G], rstd[:, 0:G]))
                for u in range(G):
                    dve.wait_ge(s_tr2, g * G + u + 1)
                    V.tensor_scalar(xr[:, u, :], acc_t[:, g * G + u, :], mv[:, u, 0:1], rstd[:, u:u + 1],
                                    ALU.subtract, ALU.mult).then_inc(s_n2, 1)

            dve.wait_ge(s_gw, 80)
            dve.wait_ge(s_logit, NT + 1)
            lg, pick1, pick2, work, comb_g = gate
            m1, m2, gap, ex, top, wt = (gcol[:, c, :] for c in range(6))

            def by_tile(v):
                return v.unsqueeze(2).to_broadcast([P, NT, NE])

            def by_expert(v):
                return v.unsqueeze(1).to_broadcast([P, NT, NE])

            def pick_largest(picked, largest):
                link(V.tensor_reduce(largest, lg, AX.X, ALU.max))
                link(V.tensor_tensor(work, lg, by_tile(largest), ALU.is_equal))
                link(V.tensor_tensor(work, work, by_expert(iota_e[:, :]), ALU.mult))
                link(V.tensor_reduce(top, work, AX.X, ALU.max))
                link(V.tensor_tensor(picked, work, by_tile(top), ALU.is_equal))

            link(V.tensor_tensor(lg, ps_root[:, 0:NT * NE].rearrange("p (t e) -> p t e", e=NE),
                                 by_expert(gvec[:, 0, :]), ALU.add))
            link(V.tensor_tensor(lg, lg, by_expert(gvec[:, 1, :]), ALU.add))
            pick_largest(pick1, m1)
            link(V.scalar_tensor_tensor(lg, pick1, -3.0e38, lg, ALU.mult, ALU.add))
            pick_largest(pick2, m2)
            V.tensor_tensor(gap, m2, m1, ALU.subtract).then_inc(s_gap, 1)
            dve.wait_ge(s_exp, 1)
            link(V.tensor_scalar(wt, ex, 1.0, None, ALU.add))
            link(V.reciprocal(wt, wt))
            link(V.tensor_tensor(ex, ex, wt, ALU.mult))
            link(V.tensor_tensor(pick1, pick1, by_tile(wt), ALU.mult))
            link(V.tensor_tensor(pick2, pick2, by_tile(ex), ALU.mult))
            link(V.tensor_tensor(comb_g, pick1, pick2, ALU.add))
            comb = comb_g.rearrange("p t e -> p (t e)")

            with dve.Fori(0, NE) as e:
                with dve.Fori(0, NG) as g:
                    for u in range(G):
                        n = (e * NG + g) * G + u
                        t = g * G + u
                        dve.wait_ge(s_y, n + 1)
                        V.tensor_tensor(ycopy[:, u, :], ps_a[u % 2][:, 0:D],
                                        b2_b.rearrange("p e d -> p (e d)")[:, ds(e * D, D)], ALU.add)\
                            .then_inc(s_yc, 1)
                        dve.wait_ge(s_yc, n + 2)
                        V.scalar_tensor_tensor(acc[:, ds(t * D, D)], ycopy[:, u, :], comb[:, ds(t * NE + e, 1)],
                                               acc[:, ds(t * D, D)], ALU.mult, ALU.add).then_inc(s_res, 1)

        @block.tensor
        def _(pe):
            T = nc.tensor
            T.sem_inc(s_tr, UD)
            T.sem_inc(s_tr2, G)
            T.sem_inc(s_logit, 1)
            T.sem_inc(s_moved, UP)
            T.sem_inc(s_sum, UA)
            pe.wait_ge(s_const, 9)

            def dense(l):
                with pe.Fori(0, JD) as j:
                    def turn(u):
                        n = l * NT + j * UD + u
                        pe.wait_ge(s_row, n + 1)
                        pe.wait_ge(s_xt, n + 1)
                        for k in range(KD):
                            i = T.transpose(ps_x[:, k * P:(k + 1) * P],
                                            xr[:, u, k * P:(k + 1) * P], ident[:, :])
                        i.then_inc(s_tr, 1)

                    def multiply(u):
                        n = l * NT + j * UD + u
                        if u == 0:
                            pe.wait_ge(s_w, (l + 1) * (16 * 2 * KD))
                        pe.wait_ge(s_xt, n + 2)
                        for q in range(TU):
                            pe.wait_ge(s_copied, n * TU + (q + 1))
                            for k in range(KD):
                                i = T.matmul(ps_t[q][:, :], xt[:, u, k, :],
                                             wr[:, k, q * R // TU:(q + 1) * R // TU, :].rearrange("p r d -> p (r d)"),
                                             start=(k == 0), stop=(k == KD - 1))
                            i.then_inc(s_unit, 1)
                        pe.wait_ge(s_rootc, n + 1)
                        for k in range(KD):
                            i = T.matmul(ps_root[:, 0:D], xt[:, u, k, :], wroot[:, k, :],
                                         start=(k == 0), stop=(k == KD - 1))
                        i.then_inc(s_root, 1)
                    turn(0)
                    for u in range(1, UD):
                        turn(u)
                        multiply(u - 1)
                    multiply(UD - 1)

            def aggregate(l):
                with pe.Fori(0, NC // UA) as j:
                    for u in range(UA):
                        n = l * NC + j * UA + u
                        pe.wait_ge(s_got[u], (l * (NC // UA) + (j + 1)) * 16)
                        pe.wait_ge(s_oh, n + 1)
                        pe.wait_ge(s_add, n + 1)
                        T.matmul(ps_a[u % 2][:, 0:D], onehot[:, u, :], msg[:, u, :], start=True, stop=True)\
                            .then_inc(s_sum, 1)

            dense(0)
            pe.wait_ge(s_cnt, 1)
            counts = small[0:EP, NT:2 * NT]
            T.matmul(ps_a[0][:, 0:NT], tri[0:EP, :], counts, start=True, stop=True)
            T.matmul(ps_a[0][:, NT:2 * NT], ones[0:EP, :], counts, start=True, stop=True).then_inc(s_base, 1)
            pe.wait_ge(s_pick, 1)
            for d in range(2):
                T.matmul(ps_a[d][:, 0:NC], zero16[:, :], iota_c[:, :], start=True, stop=False)
            with pe.Fori(0, ET // UP) as j:
                for u in range(UP):
                    pe.wait_ge(s_pick, j * UP + (u + 1))
                    for d in range(2):
                        i = T.matmul(ps_a[d][:, 0:NC], pick_s[:, u, d, :], pick_c[:, u, :], start=False, stop=False)
                    i.then_inc(s_moved, 1)
            for d in range(2):
                i = T.matmul(ps_a[d][:, 0:NC], zero16[:, :], iota_c[:, :], start=False, stop=True)
            i.then_inc(s_sorted, 1)

            aggregate(0)

            def later(l):
                dense(l)
                aggregate(l)
            layers_after_first(pe, later)

            pe.wait_ge(s_gw, 80)
            pe.wait_ge(s_rootc, L * NT + 1)
            with pe.Fori(0, NG) as g:
                def turn(u):
                    t = g * G + u
                    pe.wait_ge(s_n2, t + 1)
                    pe.wait_ge(s_tt, t + 1)
                    for k in range(KD):
                        i = T.transpose(ps_x[:, k * P:(k + 1) * P],
                                        xr[:, u, k * P:(k + 1) * P], ident[:, :])
                    i.then_inc(s_tr2, 1)

                def logits(u):
                    t = g * G + u
                    pe.wait_ge(s_tt, t + 2)
                    for k in range(KD):
                        i = T.matmul(ps_root[:, ds(t * NE, NE)], xt[:, u, k, :], wg_s[:, k, :],
                                     start=(k == 0), stop=(k == KD - 1))
                    i.then_inc(s_logit, 1)
                turn(0)
                for u in range(1, G):
                    turn(u)
                    logits(u - 1)
                logits(G - 1)
            pe.wait_ge(s_tok, NT + 1)

            def expert(e, rounds, b):
                with pe.Fori(0, NG) as g:
                    item = e * NG + g
                    pe.wait_ge(s_ew[b], (rounds + 1) * 32)
                    for half in range(2):
                        for m in range(KH):
                            q = half * KH + m
                            pe.wait_ge(s_hc, item * (2 * KH) + (q + 1))
                            for k in range(KD):
                                i = T.matmul(ps_t[m][:, 0:HB], w1_s[:, b, k, m * P:(m + 1) * P],
                                             tokT[:, k, ds(g * (G * P) + half * HB, HB)],
                                             start=(k == 0), stop=(k == KD - 1))
                            i.then_inc(s_h, 1)
                    for u in range(G):
                        n = item * G + u
                        halves = 1 if (u + 1) * P <= HB else 2
                        pe.wait_ge(s_hc, item * (2 * KH) + (KH + halves * KH))
                        pe.wait_ge(s_yc, n + 1 if u == 0 else n)
                        for m in range(KH):
                            i = T.matmul(ps_a[u % 2][:, 0:D], hT[:, m, u * P:(u + 1) * P], w2_s[:, b, m, :],
                                         start=(m == 0), stop=(m == KH - 1))
                        i.then_inc(s_y, 1)

            with pe.Fori(0, NE // 2) as pair:
                for b in range(2):
                    expert(pair * 2 + b, pair, b)


_INS = ['x', 'src', 'dst', 'edge_type_8', 'L0_gnn_W_rel', 'L0_gnn_W_root', 'L0_gnn_bias', 'L0_ffn_Wg', 'L0_ffn_bg',
        'L0_ffn_bias', 'L0_ffn_W1', 'L0_ffn_b1', 'L0_ffn_W2', 'L0_ffn_b2']
_OUTS = [((3125, 256), 'float32')]


def kernel(**inputs):
    import numpy as _np
    import concourse.bacc as _bacc
    from concourse import mybir as _mybir
    from concourse.bass_utils import run_bass_kernel_spmd as _run

    nc = _bacc.Bacc("TRN2", target_bir_lowering=False, num_devices=1)
    arrays, args = {}, []
    for name in _INS:
        a = _np.ascontiguousarray(inputs[name])
        arrays[f"in_{name}_dram"] = a
        args.append(nc.dram_tensor(f"in_{name}_dram", a.shape, _mybir.dt.from_np(a.dtype), kind="ExternalInput").ap())
    for i, (shape, dtype) in enumerate(_OUTS):
        dt = _mybir.dt.from_np(_np.dtype(dtype))
        args.append(nc.dram_tensor(f"out_{i}_dram", shape, dt, kind="ExternalOutput").ap())
    build_rgcn_moe(nc, *args)
    r = _run(nc, [arrays], core_ids=[0])
    got = tuple(r.results[0][f"out_{i}_dram"] for i in range(len(_OUTS)))
    return got[0]
```
